# Optimizing a Trainium2 kernel written in Bass

```python
import numpy as np
import jax
import jax.numpy as jnp

def _softmax(x, axis=-1):
    return jax.nn.softmax(x, axis=axis)

def _gelu(x):
    return jax.nn.gelu(x, approximate=True)

def _silu(x):
    return jax.nn.silu(x)

def _sigmoid(x):
    return jax.nn.sigmoid(x)

def _layernorm(x, axis=-1, eps=1e-05):
    m = jnp.mean(x, axis=axis, keepdims=True)
    v = jnp.var(x, axis=axis, keepdims=True)
    return (x - m) / jnp.sqrt(v + eps)

def _scatter_add(tgt, idx, src, axis=0):
    return tgt.at[idx].add(src)

def _segment_sum(src, seg, n):
    return jax.ops.segment_sum(src, seg, n)
kernel_name = 'mk_flamingo_gated_d1_seqx_r4_9a58f6'

def setup_inputs(seed: int=0):
    np.random.seed(seed)
    _w = jnp.asarray

    def _rec_inputs():
        import jax
        import jax.numpy as jnp
        _rk = jax.random.key(seed)
        x = -0.0002928 + 1 * jax.random.normal(jax.random.fold_in(_rk, 1), (32, 256, 256), jnp.float32)
        _lenS = 256 - jax.random.randint(jax.random.fold_in(_rk, 7), (32,), 0, max(1, 256 // 4) + 1, jnp.int32)
        _lenS2 = 256 - jax.random.randint(jax.random.fold_in(_rk, 8), (32,), 0, max(1, 256 // 4) + 1, jnp.int32)
        _ctx_1024P = jax.random.normal(jax.random.fold_in(_rk, 11), (32, 16, 256), jnp.float32)
        _ctx_1024c = jax.random.dirichlet(jax.random.fold_in(_rk, 511), 0.3 * jnp.ones((16,), jnp.float32), (32, 256))
        _ctx_1024t = jnp.einsum('bsk,bkd->bsd', _ctx_1024c, _ctx_1024P)
        _ctx_1024t = _ctx_1024t * jax.lax.rsqrt(jnp.mean(jnp.square(_ctx_1024t)) + 1e-12) * 0.953939
        ctx_1024 = -1.39393e-06 + 0.999914 * (_ctx_1024t + 0.3 * jax.random.normal(jax.random.fold_in(_rk, 611), (32, 256, 256), jnp.float32))
        _g = jax.random.normal(jax.random.fold_in(_rk, 9001), (2, 1), jnp.float32)
        _g = jnp.sign(_g) * jnp.maximum(jnp.abs(_g), 1.0) + (_g == 0) * 1.0
        g_xattn = _g[0]
        g_ffn = _g[1]
        return (x, ctx_1024, g_xattn, g_ffn)
    x, ctx_1024, g_xattn, g_ffn = _rec_inputs()

    def _L0_xattn_setup():
        import jax, jax.numpy as jnp
        import numpy as np
        EMBED_DIM = 256
        NUM_HEADS = 16
        HEAD_DIM = EMBED_DIM // NUM_HEADS

        def _split_heads(x, B, S):
            return x.reshape(B, S, NUM_HEADS, HEAD_DIM).transpose(0, 2, 1, 3)
        key = jax.random.key(seed)
        ks = jax.random.split(key, 11)
        B, S, D = (2, 512, EMBED_DIM)
        scale = 1.0 / np.sqrt(D)
        inp = {'query': jax.random.normal(ks[0], (B, S, D), jnp.float32), 'key': jax.random.normal(ks[1], (B, S, D), jnp.float32), 'value': jax.random.normal(ks[2], (B, S, D), jnp.float32), 'Wq': jax.random.normal(ks[3], (D, D), jnp.float32) * scale, 'bq': jnp.zeros((D,), jnp.float32), 'Wk': jax.random.normal(ks[4], (D, D), jnp.float32) * scale, 'bk': jnp.zeros((D,), jnp.float32), 'Wv': jax.random.normal(ks[5], (D, D), jnp.float32) * scale, 'bv': jnp.zeros((D,), jnp.float32), 'Wo': jax.random.normal(ks[6], (D, D), jnp.float32) * scale, 'bo': jnp.zeros((D,), jnp.float32)}
        return inp
    _L0_xattn_all = _L0_xattn_setup()
    _L0_xattn_in = {k: v for k, v in _L0_xattn_all.items() if k in ('Wq', 'bq', 'Wk', 'bk', 'Wv', 'bv', 'Wo', 'bo')}
    del _L0_xattn_all

    def _L0_ffn_setup():
        import jax, jax.numpy as jnp
        import numpy as np
        E = 8
        K = 2
        CF = 1.25
        key = jax.random.key(seed)
        kx, kr, kg, ku, kd = jax.random.split(key, 5)
        D, F = (256, 1024)
        x = jax.random.normal(kx, (4, 512, D), dtype=jnp.float32)
        router_w = 0.02 * jax.random.normal(kr, (E, D), dtype=jnp.float32)
        wg = jax.random.normal(kg, (E, D, F), dtype=jnp.float32) / np.sqrt(D)
        wu = jax.random.normal(ku, (E, D, F), dtype=jnp.float32) / np.sqrt(D)
        wd = jax.random.normal(kd, (E, F, D), dtype=jnp.float32) / np.sqrt(F)
        return {'x': x, 'router_w': router_w, 'wg': wg, 'wu': wu, 'wd': wd}
    _L0_ffn_all = _L0_ffn_setup()
    _L0_ffn_in = {k: v for k, v in _L0_ffn_all.items() if k in ('router_w', 'wg', 'wu', 'wd')}
    del _L0_ffn_all
    return {'x': x, 'ctx_1024': ctx_1024, 'g_xattn': g_xattn, 'g_ffn': g_ffn, 'L0_xattn_Wq': _L0_xattn_in['Wq'], 'L0_xattn_bq': _L0_xattn_in['bq'], 'L0_xattn_Wk': _L0_xattn_in['Wk'], 'L0_xattn_bk': _L0_xattn_in['bk'], 'L0_xattn_Wv': _L0_xattn_in['Wv'], 'L0_xattn_bv': _L0_xattn_in['bv'], 'L0_xattn_Wo': _L0_xattn_in['Wo'], 'L0_xattn_bo': _L0_xattn_in['bo'], 'L0_ffn_router_w': _L0_ffn_in['router_w'], 'L0_ffn_wg': _L0_ffn_in['wg'], 'L0_ffn_wu': _L0_ffn_in['wu'], 'L0_ffn_wd': _L0_ffn_in['wd']}

def reference(x, ctx_1024, g_xattn, g_ffn, L0_xattn_Wq, L0_xattn_bq, L0_xattn_Wk, L0_xattn_bk, L0_xattn_Wv, L0_xattn_bv, L0_xattn_Wo, L0_xattn_bo, L0_ffn_router_w, L0_ffn_wg, L0_ffn_wu, L0_ffn_wd):
    import jax
    import jax.numpy as jnp

    def _L0_xattn_ref(query, key, value, Wq, bq, Wk, bk, Wv, bv, Wo, bo):
        import jax, jax.numpy as jnp
        import numpy as np
        EMBED_DIM = 256
        NUM_HEADS = 16
        HEAD_DIM = EMBED_DIM // NUM_HEADS

        def _split_heads(x, B, S):
            return x.reshape(B, S, NUM_HEADS, HEAD_DIM).transpose(0, 2, 1, 3)
        B, S, D = query.shape
        q = _split_heads(query @ Wq + bq, B, S)
        k = _split_heads(key @ Wk + bk, B, S)
        v = _split_heads(value @ Wv + bv, B, S)
        score = jnp.einsum('bhqd,bhkd->bhqk', q, k) / np.sqrt(HEAD_DIM)
        weights = jax.nn.softmax(score, axis=-1)
        attn = jnp.einsum('bhqk,bhkd->bhqd', weights, v)
        out = attn.transpose(0, 2, 1, 3).reshape(B, S, D)
        return out @ Wo + bo

    def _L0_ffn_ref(x, router_w, wg, wu, wd):
        import jax, jax.numpy as jnp
        import numpy as np
        E = 8
        K = 2
        CF = 1.25
        B, L, D = x.shape
        xf = x.reshape(-1, D)
        N = xf.shape[0]
        capacity = max(1, int(CF * N / E))
        logits = xf @ router_w.T
        probs = jax.nn.softmax(logits, axis=-1)
        topw, topi = jax.lax.top_k(probs, K)
        topw = topw / (topw.sum(-1, keepdims=True) + 1e-06)
        fe = topi.reshape(-1)
        fw = topw.reshape(-1)
        ft = jnp.repeat(jnp.arange(N), K)
        order = jnp.lexsort((-fw, fe))
        se, sw, st = (fe[order], fw[order], ft[order])
        counts = jax.ops.segment_sum(jnp.ones_like(se), se, num_segments=E)
        starts = jnp.cumsum(counts) - counts
        rank = jnp.arange(N * K) - starts[se]
        keep = rank < capacity
        pos = jnp.where(keep, rank, capacity)
        disp = jnp.zeros((E, capacity + 1, D), x.dtype).at[se, pos].set(xf[st])
        disp = disp[:, :capacity]
        g = jnp.einsum('ecd,edf->ecf', disp, wg)
        u = jnp.einsum('ecd,edf->ecf', disp, wu)
        eo = jnp.einsum('ecf,efd->ecd', jax.nn.silu(g) * u, wd)
        gathered = eo[se, jnp.minimum(pos, capacity - 1)]
        contrib = gathered * (sw * keep.astype(x.dtype))[:, None]
        out = jnp.zeros_like(xf).at[st].add(contrib)
        return out.reshape(B, L, D)
    x = x + jnp.tanh(g_xattn[0]) * _L0_xattn_ref(_layernorm(x, axis=-1), ctx_1024, ctx_1024, L0_xattn_Wq, L0_xattn_bq, L0_xattn_Wk, L0_xattn_bk, L0_xattn_Wv, L0_xattn_bv, L0_xattn_Wo, L0_xattn_bo)
    x = x + jnp.tanh(g_ffn[0]) * _L0_ffn_ref(_layernorm(x, axis=-1), L0_ffn_router_w, L0_ffn_wg, L0_ffn_wu, L0_ffn_wd)
    return x

_drawn_inputs = setup_inputs


def setup_inputs(seed=0):
    import zlib

    import numpy as np

    out = dict(_drawn_inputs(seed))
    spreads = {'L0_xattn_bq': (0.0, 0.1),
     'L0_xattn_bk': (0.0, 0.1),
     'L0_xattn_bv': (0.0, 0.1),
     'L0_xattn_bo': (0.0, 0.1)}
    factors = {}
    for name, (base, spread) in spreads.items():
        noise = np.random.default_rng([zlib.crc32(name.encode()), seed]).standard_normal(out[name].shape)
        drawn = base * np.exp(spread * noise) if base else spread * noise
        out[name] = jnp.asarray(drawn.astype(out[name].dtype))
    for name, factor in factors.items():
        out[name] = (out[name] * factor).astype(out[name].dtype)
    return out
```

```python
from contextlib import ExitStack

import concourse.bass as bass
from concourse import mybir

P = 128
F32 = mybir.dt.float32
F16 = mybir.dt.float16
I32 = mybir.dt.int32
U32 = mybir.dt.uint32
ALU = mybir.AluOpType
ACT = mybir.ActivationFunctionType
AX_X = mybir.AxisListType.X

B, S, D = 32, 256, 256
H, HD = 16, 16
N = B * S
E, F = 8, 1024
K = 2
CAP = int(1.25 * N / E)
T = N // P
TC = S // P
KC = D // P
HM = H // KC
FC = F // P
EPS = 1e-5
QK_SCALE = 16.0
M_SCALE = QK_SCALE * QK_SCALE
SM_SCALE = 1.0 / HD ** 0.5
KROWS = 96
MROW = KROWS
ROW = D + E
SPARE = P
SLOTS = CAP // P
KEPT = 100.0



PRO, TRIPS, NBUF = 6, 8, 3
LAG_B, LAG_C, LAG_D = 1, 2, 4
STEPS = B + LAG_D + 1
T_USES = (0, 0, LAG_D)
P_USES = (0, 0, LAG_D, LAG_B)
M_USES = (LAG_B + 1, LAG_D + 1, LAG_B)


def due(n):
    return not isinstance(n, int) or n > 0


def active(i, lag):
    return not isinstance(i, int) or 0 <= i - lag < B


def uses(i, lags, k):
    if isinstance(i, int):
        return sum(min(max(i - lag, 0), B) for lag in lags) + sum(active(i, lag) for lag in lags[:k])
    return i * len(lags) + (k - sum(lags))


def run(eng, step):
    for i in range(PRO):
        step(i, i % NBUF, i // NBUF)
    with eng.Fori(0, TRIPS) as trip:
        for r in range(NBUF):
            step(trip * NBUF + (PRO + r), r, trip + PRO // NBUF)
    for i in range(PRO + TRIPS * NBUF, STEPS):
        step(i, i % NBUF, i // NBUF)


def lagged(r, turn, lag):
    q = (r - lag) // NBUF
    return (r - lag) % NBUF, turn + q


def wide(ap, n):
    return ap.unsqueeze(1).to_broadcast([ap.shape[0], n, ap.shape[1]])


def attention(nc, dram, wsel, ident, raw):
    x, ctx, out, rows, rsum, rinv = (dram[k] for k in ("x", "ctx", "out", "rows", "rsum", "rinv"))
    NPT = 4

    with ExitStack() as es:
        def sb(name, shape, dt=F32):
            return es.enter_context(nc.sbuf_tensor(name, shape, dt))

        def pb(name):
            return es.enter_context(nc.psum_tensor(name, [P, 512], F32))

        def sem(name):
            return es.enter_context(nc.semaphore(name))

        wq_sb = sb("wq_sb", [P, KC, D])
        wk_sb = sb("wk_sb", [P, KC, D])
        wq_raw = sb("wq_raw", [P, KC, D])
        wk_raw = sb("wk_raw", [P, KC, D])
        wv_sb = sb("wv_sb", [P, KC, D])
        wo_sb = sb("wo_sb", [P, KC, D])
        rt_rows = sb("rt_rows", [E, D])
        rt_sb = sb("rt_sb", [P, KC, E])
        bq_raw = sb("bq_raw", [P, KC])
        bk_raw = sb("bk_raw", [P, KC])
        bq_sb = sb("bq_sb", [P, KC])
        bk_sb = sb("bk_sb", [P, KC])
        bv_sb = sb("bv_sb", [P, D])
        bo_sb = sb("bo_sb", [P, D])
        bo_g = sb("bo_g", [P, D])
        g_raw = sb("g_raw", [P, 1])
        g_tanh = sb("g_tanh", [P, 1])
        iota_e = sb("iota_e", [P, E])
        eps_sb = sb("eps_sb", [P, TC])
        mhalf = sb("mhalf", [P, TC])
        xt = sb("xt", [P, NBUF, TC, D])
        ct = sb("ct", [P, NBUF, TC, D])
        st1 = sb("st1", [P, TC, 6])
        mv1 = sb("mv1", [P, TC, 2])
        ve1 = sb("ve1", [P, TC])
        rs1 = sb("rs1", [P, TC])
        z = sb("z", [P, TC, D])
        zT = sb("zT", [P, KC, S])
        cT = sb("cT", [P, NBUF, KC, S])
        q32 = sb("q32", [P, KC, S])
        k32 = sb("k32", [P, KC, S])
        qh = sb("qh", [P, KC, S], F16)
        ql = sb("ql", [P, KC, S], F16)
        kh = sb("kh", [P, KC, S], F16)
        kl = sb("kl", [P, KC, S], F16)
        qa = [sb(f"qa{n}", [P, HM, KC, S], F16) for n in range(NBUF)]
        ka = [sb(f"ka{n}", [P, HM, KC, S], F16) for n in range(NBUF)]
        va = sb("va", [P, NBUF, TC, H, 2 * HD])
        mx = sb("mx", [P, TC, H])
        mrow = sb("mrow", [HM, KC, S], F16)
        pT = sb("pT", [P, NPT, TC, S])
        u = sb("u", [P, 4, S])
        den = sb("den", [P, H * S // P])
        rec = sb("rec", [P, H * S // P])
        uc = sb("uc", [P, NBUF, KC, S])
        rb = sb("rb", [P, NBUF, KC, S])
        xr = sb("xr", [P, TC, D])
        xb = sb("xb", [P, TC, D])
        an = sb("an", [P, KC, S])
        x1 = sb("x1", [P, TC, D])
        st2 = sb("st2", [P, TC, 6])
        mv2 = sb("mv2", [P, TC, 2])
        ve2 = sb("ve2", [P, TC])
        rs2 = sb("rs2", [P, TC])
        zr = sb("zr", [P, TC, ROW])
        z2T = sb("z2T", [P, KC, S])
        top = sb("top", [P, TC, 8])
        tix = sb("tix", [P, TC, 8], U32)
        tif = sb("tif", [P, TC, K])
        ntop = sb("ntop", [P, TC])
        ex = sb("ex", [P, TC, 8])
        esum = sb("esum", [P, TC])
        dn0 = sb("dn0", [P, TC])
        dn = sb("dn", [P, TC])
        w12 = sb("w12", [P, TC, K])
        oh = sb("oh", [P, K, TC, E])
        ow = sb("ow", [P, K, TC, E])
        hit = sb("hit", [P, TC, E])

        ps_t = pb("ps_t")
        ps_p = pb("ps_p")
        ps_m = pb("ps_m")
        ps_s = [pb(f"ps_s{n}") for n in range(2)]
        ps_k = [pb(f"ps_k{n}") for n in range(2)]
        ps_v = pb("ps_v")

        const_in = sem("const_in")
        wo_in = sem("wo_in")
        const_pool = sem("const_pool")
        const_dve = sem("const_dve")
        gate_ready = sem("gate_ready")
        waited = sem("waited")
        fixed = [sem(f"fixed{n}") for n in range(NBUF)]
        mrow_set = sem("mrow_set")
        raw_in0 = sem("raw_in0")
        router_tp = sem("router_tp")
        t_mm, t_out = sem("t_mm"), sem("t_out")
        p_mm, p_out = sem("p_mm"), sem("p_out")
        m_mm, m_out = sem("m_mm"), sem("m_out")
        x_in = [sem(f"x_in{n}") for n in range(NBUF)]
        c_in = [sem(f"c_in{n}") for n in range(NBUF)]
        st1_done = sem("st1_done")
        mv1_done = sem("mv1_done")
        ve1_done = sem("ve1_done")
        rs1_done = sem("rs1_done")
        z_done = sem("z_done")
        qh_done = sem("qh_done")
        kh_done = sem("kh_done")
        ql_done = sem("ql_done")
        kl_done = sem("kl_done")
        q_stack = sem("q_stack")
        k_stack = sem("k_stack")
        s_mm = sem("s_mm")
        mx_done = sem("mx_done")
        m_stack = [sem(f"m_stack{n}") for n in range(2)]
        k_sc = sem("k_sc")
        p_done = sem("p_done")
        pv_done = sem("pv_done")
        u_done = sem("u_done")
        uc_in = sem("uc_in")
        den_out = sem("den_out")
        den_in = sem("den_in")
        rec_done = sem("rec_done")
        rec_out = sem("rec_out")
        rb_in = sem("rb_in")
        xr_in = sem("xr_in")
        xb_done = sem("xb_done")
        an_done = sem("an_done")
        x1_done = sem("x1_done")
        x1_out = sem("x1_out")
        st2_done = sem("st2_done")
        mv2_done = sem("mv2_done")
        ve2_done = sem("ve2_done")
        rs2_done = sem("rs2_done")
        z2_done = sem("z2_done")
        top_done = sem("top_done")
        tix_done = sem("tix_done")
        tif_done = sem("tif_done")
        ntop_done = sem("ntop_done")
        ex_done = sem("ex_done")
        dn0_done = sem("dn0_done")
        dn_done = sem("dn_done")
        w1_done = sem("w1_done")
        w2_done = sem("w2_done")
        oh_done = sem("oh_done")
        ow_done = sem("ow_done")
        hit_done = sem("hit_done")
        wt_done = sem("wt_done")
        wsel_done = sem("wsel_done")
        rows_out = sem("rows_out")

        N_CONST = 16 * (3 + 1 + 2 * KC + 3)
        POOL_CONSTS = 6
        FIXED = 2
        DVE_CONSTS = 6

        def token_rows(t, b, width):
            return t[bass.ts(b, TC), :, 0:width].rearrange("c p n -> p c n")

        block = es.enter_context(nc.Block())

        def alone(eng):
            eng.sem_inc(waited, 1)

        @block.sync
        def _(sp):
            for n in range(2):
                sp.dma_start(xt[:, n, :, :], token_rows(x, n, D)).then_inc(x_in[n], 16)
            sp.dma_start(ct[:, 0, :, :], token_rows(ctx, 0, D)).then_inc(c_in[0], 16)
            for dst, src in ((wq_raw, dram["wq"]), (wk_raw, dram["wk"]), (wv_sb, dram["wv"])):
                sp.dma_start(dst[:], src.rearrange("(c p) n -> p c n", p=P)).then_inc(const_in, 16)
            sp.dma_start(rt_rows[:], dram["router"]).then_inc(const_in, 16)
            with nc.allow_non_contiguous_dma(reason="256 bias values onto partitions, once"):
                for dst, src in ((bq_raw, dram["bq"]), (bk_raw, dram["bk"])):
                    for a in range(KC):
                        sp.dma_start(dst[:, a:a + 1], src[a * P:(a + 1) * P].rearrange("(m d) -> d m", m=HM)
                                     .unsqueeze(2)).then_inc(const_in, 16)
            for dst, src in ((bv_sb, dram["bv"]), (bo_sb, dram["bo"]), (g_raw, dram["g_xattn"])):
                sp.dma_start(dst[:], src.partition_broadcast(P)).then_inc(const_in, 16)

            def step(i, r, turn):
                if active(i, -2):
                    if due(i):
                        sp.wait_ge(z_done, i)
                    alone(sp)
                    sp.dma_start(xt[:, (r + 2) % NBUF, :, :], token_rows(x, i + 2, D)).then_inc(x_in[(r + 2) % NBUF], 16)
                if active(i, -1):
                    if due(i - 1):
                        sp.wait_ge(t_mm, uses(i - 2, T_USES, 1) + 1)
                    alone(sp)
                    sp.dma_start(ct[:, (r + 1) % NBUF, :, :], token_rows(ctx, i + 1, D)).then_inc(c_in[(r + 1) % NBUF], 16)
                if active(i, LAG_C + 1):
                    b = i - LAG_C - 1
                    rr, _ = lagged(r, turn, LAG_C + 1)
                    sp.wait_ge(u_done, 2 * b + 2)
                    for g in range(2):
                        sp.dma_start(rsum.rearrange("(j a c q) -> a j c q", j=4, a=2, c=KC)[g],
                                     u[HD:P:32, g:4:2, :]).then_inc(den_out, 16)
                    if due(b - 2):
                        sp.wait_ge(an_done, b - 2)
                    for g in range(2):
                        for j in range(4):
                            p0 = 32 * j + HD * g
                            sp.dma_start(uc[p0:p0 + HD, rr, :, :], u[32 * j:32 * j + HD, g:4:2, :]).then_inc(uc_in, 16)
                    sp.wait_ge(den_out, 32 * (b + 1))
                    if due(b):
                        sp.wait_ge(rec_done, b)
                    alone(sp)
                    sp.dma_start(den[:], rsum.rearrange("(p n) -> p n", p=P)).then_inc(den_in, 16)
                if active(i, LAG_B + 1):
                    b = i - LAG_B - 1
                    rr, _ = lagged(r, turn, LAG_B + 1)
                    sp.wait_ge(m_out, uses(i, M_USES, 0) + 1)
                    alone(sp)
                    sp.dma_start(qa[rr][MROW:MROW + 1, :, 1, :], mrow[:, 1, :]).then_inc(m_stack[1], 16)
                if active(i, LAG_D - 1):
                    b = i - LAG_D + 1
                    if due(b):
                        sp.wait_ge(xb_done, b)
                    alone(sp)
                    sp.dma_start(xr[:], token_rows(x, b, D)).then_inc(xr_in, 16)
                if active(i, 0):
                    sp.wait_ge(qh_done, i + 1)
                    alone(sp)
                    if isinstance(i, int) and i < NBUF:
                        sp.wait_ge(fixed[i], FIXED)
                        sp.wait_ge(mrow_set, NBUF)
                    if due(i - 2):
                        sp.wait_ge(k_sc, H * (i - 2))
                    alone(sp)
                    sp.dma_start(qa[r][0:HD, :, :, :], qh[:]).then_inc(q_stack, 16)
                    sp.dma_start(qa[r][2 * HD:3 * HD, :, :, :], qh[:]).then_inc(q_stack, 16)
                    sp.wait_ge(ql_done, i + 1)
                    alone(sp)
                    sp.dma_start(qa[r][HD:2 * HD, :, :, :], ql[:]).then_inc(q_stack, 16)
                if active(i, 0):
                    sp.wait_ge(kh_done, i + 1)
                    alone(sp)
                    sp.dma_start(ka[r][0:HD, :, :, :], kh[:]).then_inc(k_stack, 16)
                    sp.dma_start(ka[r][HD:2 * HD, :, :, :], kh[:]).then_inc(k_stack, 16)
                    sp.wait_ge(kl_done, i + 1)
                    alone(sp)
                    sp.dma_start(ka[r][2 * HD:3 * HD, :, :, :], kl[:]).then_inc(k_stack, 16)
                if active(i, LAG_D + 1):
                    b = i - LAG_D - 1
                    sp.wait_ge(wt_done, b + 1)
                    alone(sp)
                    sp.dma_start(token_rows(rows, b, ROW), zr[:]).then_inc(rows_out, 16)
                if active(i, LAG_D):
                    b = i - LAG_D
                    sp.wait_ge(x1_done, b + 1)
                    alone(sp)
                    sp.dma_start(token_rows(out, b, D), x1[:]).then_inc(x1_out, 16)
                if active(i, LAG_B):
                    rr, _ = lagged(r, turn, LAG_B)
                    sp.wait_ge(m_out, uses(i, M_USES, 2) + 1)
                    alone(sp)
                    sp.dma_start(qa[rr][MROW:MROW + 1, :, 0, :], mrow[:, 0, :]).then_inc(m_stack[0], 16)
                if active(i, LAG_C + 1):
                    b = i - LAG_C - 1
                    rr, _ = lagged(r, turn, LAG_C + 1)
                    sp.wait_ge(rec_done, b + 1)
                    alone(sp)
                    if due(b):
                        sp.wait_ge(rb_in, 16 * b)
                    alone(sp)
                    sp.dma_start(rinv.rearrange("(p n) -> p n", p=P), rec[:]).then_inc(rec_out, 16)
                    sp.wait_ge(rec_out, 16 * (b + 1))
                    alone(sp)
                    sp.dma_start(rb[:, rr, :, :], rinv.rearrange("(j n) -> j n", j=8).unsqueeze(1)
                                 .to_broadcast([8, HD, KC * S])).then_inc(rb_in, 16)

                if isinstance(i, int) and B <= i < B + PREP:
                    load_weights(sp, dram, raw, 0, i - B, raw_in0)

            run(sp, step)
            sp.wait_ge(raw_in0, 48)
            sp.wait_ge(x1_out, 16 * B)
            sp.wait_ge(rows_out, 16 * B)

        @block.gpsimd
        def _(pool):
            nc.gpsimd.memset(ident[:], 0.0).then_inc(const_pool, 1)
            pool.wait_ge(const_pool, 1)
            nc.gpsimd.affine_select(out=ident[:], in_=ident[:], compare_op=ALU.not_equal, fill=1.0, base=0,
                                    pattern=[[-1, P]], channel_multiplier=1).then_inc(const_pool, 1)
            nc.gpsimd.iota(iota_e[:], [[1, E]], base=0, channel_multiplier=0,
                           allow_small_or_imprecise_dtypes=True).then_inc(const_pool, 1)
            nc.gpsimd.memset(eps_sb[:], EPS).then_inc(const_pool, 1)
            nc.gpsimd.memset(mhalf[:], -0.5).then_inc(const_pool, 1)
            nc.gpsimd.memset(va[:, :, :, :, HD:2 * HD], 1.0).then_inc(const_pool, 1)
            pool.wait_ge(const_pool, POOL_CONSTS)
            for n in range(NBUF):
                if n:
                    pool.wait_ge(mrow_set, n)
                nc.gpsimd.memset(ka[n][MROW:MROW + 1, :, :, :], -M_SCALE).then_inc(mrow_set, 1)
            pool.wait_ge(mrow_set, NBUF)
            pool.wait_ge(const_dve, DVE_CONSTS)

            def row_scales(b):
                pool.wait_ge(mv1_done, b + 1)
                if due(b):
                    pool.wait_ge(z_done, b)
                nc.gpsimd.tensor_tensor(ve1[:], mv1[:, :, 1], eps_sb[:], ALU.add).then_inc(ve1_done, 1)
                pool.wait_ge(ve1_done, b + 1)
                nc.gpsimd.tensor_tensor(rs1[:], ve1[:], mhalf[:], ALU.pow).then_inc(rs1_done, 1)

            row_scales(0)

            def step(i, r, turn):
                if active(i, -1):
                    row_scales(i + 1)
                if active(i, LAG_D):
                    b = i - LAG_D
                    rr, _ = lagged(r, turn, LAG_D)
                    pool.wait_ge(uc_in, 128 * (b + 1))
                    pool.wait_ge(rb_in, 16 * (b + 1))
                    if due(b):
                        pool.wait_ge(p_mm, uses(i - 1, P_USES, 2) + 1)
                    nc.gpsimd.tensor_tensor(an[:], uc[:, rr, :, :], rb[:, rr, :, :], ALU.mult).then_inc(an_done, 1)
                    pool.wait_ge(xr_in, 16 * (b + 1))
                    if due(b):
                        pool.wait_ge(x1_done, b)
                    nc.gpsimd.tensor_tensor(xb[:], xr[:], wide(bo_g[:], TC), ALU.add).then_inc(xb_done, 1)
                if active(i, 0):
                    pool.wait_ge(qh_done, i + 1)
                    if due(i):
                        pool.wait_ge(q_stack, 48 * i)
                    nc.gpsimd.tensor_tensor(ql[:], q32[:], qh[:], ALU.subtract).then_inc(ql_done, 1)
                    pool.wait_ge(kh_done, i + 1)
                    if due(i):
                        pool.wait_ge(k_stack, 48 * i)
                    nc.gpsimd.tensor_tensor(kl[:], k32[:], kh[:], ALU.subtract).then_inc(kl_done, 1)
                if active(i, LAG_D):
                    b = i - LAG_D
                    pool.wait_ge(mv2_done, b + 1)
                    if due(b):
                        pool.wait_ge(z2_done, b)
                    nc.gpsimd.tensor_tensor(ve2[:], mv2[:, :, 1], eps_sb[:], ALU.add).then_inc(ve2_done, 1)
                    pool.wait_ge(ve2_done, b + 1)
                    nc.gpsimd.tensor_tensor(rs2[:], ve2[:], mhalf[:], ALU.pow).then_inc(rs2_done, 1)

                if isinstance(i, int) and i < LAG_D:
                    for s in range(i * H // LAG_D, (i + 1) * H // LAG_D):
                        c, g, j = s // 8, (s // 4) % 2, s % 4
                        p0 = 32 * j + HD * g
                        pool.dma_start(wo_sb[p0:p0 + HD, c, :], dram["wo"][s * HD:(s + 1) * HD, :]).then_inc(wo_in, 16)

            run(pool, step)

        @block.tensor
        def _(pe):
            pe.wait_ge(const_pool, POOL_CONSTS)
            pe.wait_ge(const_in, N_CONST)
            for c in range(KC):
                last = nc.tensor.transpose(ps_m[:, c * E:(c + 1) * E], rt_rows[:, c * P:(c + 1) * P], ident[0:E, 0:E])
            last.then_inc(router_tp, 1)
            pe.wait_ge(const_dve, DVE_CONSTS)

            def transposes(src):
                for kc in range(KC):
                    for c in range(TC):
                        last = nc.tensor.transpose(ps_t[:, kc * S + c * P:kc * S + (c + 1) * P],
                                                   src[:, c, kc * P:(kc + 1) * P], ident[:])
                return last

            def step(i, r, turn):
                bB, bC, bD = i - LAG_B, i - LAG_C, i - LAG_D
                rB, _ = lagged(r, turn, LAG_B)
                rC, _ = lagged(r, turn, LAG_C)

                def free(out_sem, lags, k):
                    n = uses(i, lags, k)
                    if due(n):
                        pe.wait_ge(out_sem, n)

                def scores(s):
                    if s == 0:
                        pe.wait_ge(q_stack, 48 * (bB + 1))
                        pe.wait_ge(k_stack, 48 * (bB + 1))
                    n = H * bB + s - 1
                    if due(n):
                        pe.wait_ge(mx_done, n)
                    for c in range(TC):
                        last = nc.tensor.matmul(ps_s[s % 2][:, c * S:(c + 1) * S],
                                                qa[rB][0:KROWS, s % HM, s // HM, c * P:(c + 1) * P],
                                                ka[rB][0:KROWS, s % HM, s // HM, :], start=True, stop=True)
                    last.then_inc(s_mm, 1)

                def key_scores(s):
                    if s % HM == 0:
                        pe.wait_ge(m_stack[s // HM], 16 * (bC + 1))
                    n = H * bC + s - 1
                    if due(n):
                        pe.wait_ge(p_done, n)
                    for c in range(TC):
                        last = nc.tensor.matmul(ps_k[s % 2][:, c * S:(c + 1) * S],
                                                ka[rC][0:KROWS + 1, s % HM, s // HM, c * P:(c + 1) * P],
                                                qa[rC][0:KROWS + 1, s % HM, s // HM, :], start=True, stop=True)
                    last.then_inc(k_sc, 1)

                def p_v(s):
                    pe.wait_ge(p_done, H * bC + s + 1)
                    if s == 0:
                        pe.wait_ge(p_out, uses(i - 1, P_USES, 3) + 1)
                    n = 2 * bC + s // 8
                    if s % 8 == 0 and due(n):
                        pe.wait_ge(u_done, n)
                    j, g = s % 4, (s // 4) % 2
                    for c in range(TC):
                        last = nc.tensor.matmul(ps_v[32 * j:32 * j + 32, g * S:(g + 1) * S],
                                                va[:, rC, c, s, :], pT[:, s % NPT, c, :],
                                                start=(c == 0), stop=(c == TC - 1))
                    last.then_inc(pv_done, 1)

                def max_rows(k, half, b):
                    free(m_out, M_USES, k)
                    pe.wait_ge(mx_done, H * b + HM * (half + 1))
                    for c in range(TC):
                        last = nc.tensor.transpose(ps_m[0:HM, c * P:(c + 1) * P],
                                                   mx[:, c, half * HM:(half + 1) * HM], ident[:])
                    last.then_inc(m_mm, 1)

                for s in range(H + 2):
                    if s < H and active(i, LAG_B):
                        scores(s)
                    if s < H and active(i, LAG_C):
                        key_scores(s)
                    if s == 1 and active(i, 0):
                        pe.wait_ge(z_done, i + 1)
                        free(t_out, T_USES, 0)
                        transposes(z).then_inc(t_mm, 1)
                    if s == 2 and active(i, LAG_B + 1):
                        max_rows(0, 1, bB - 1)
                    if s == 2 and active(i, 0):
                        pe.wait_ge(t_out, uses(i, T_USES, 0) + 1)
                        free(p_out, P_USES, 0)
                        for m in range(KC):
                            for c in range(KC):
                                last = nc.tensor.matmul(ps_p[:, m * S:(m + 1) * S], wq_sb[:, c, m * P:(m + 1) * P], zT[:, c, :],
                                                        start=(c == 0), stop=(c == KC - 1))
                        last.then_inc(p_mm, 1)
                    if s == 2 and active(i, 0):
                        pe.wait_ge(c_in[r], 16 * (turn + 1))
                        free(t_out, T_USES, 1)
                        transposes(ct[:, r]).then_inc(t_mm, 1)
                    if s == 6 and active(i, 0):
                        pe.wait_ge(t_out, uses(i, T_USES, 1) + 1)
                        free(p_out, P_USES, 1)
                        for m in range(KC):
                            for c in range(KC):
                                last = nc.tensor.matmul(ps_p[:, m * S:(m + 1) * S], wk_sb[:, c, m * P:(m + 1) * P], cT[:, r, c, :],
                                                        start=(c == 0), stop=(c == KC - 1))
                        last.then_inc(p_mm, 1)
                    if s == 7 and active(i, LAG_D):
                        if isinstance(i, int) and i == LAG_D:
                            pe.wait_ge(wo_in, 16 * H)
                        pe.wait_ge(an_done, bD + 1)
                        free(p_out, P_USES, 2)
                        for c in range(TC):
                            for kc in range(KC):
                                last = nc.tensor.matmul(ps_p[:, c * D:(c + 1) * D], an[:, kc, c * P:(c + 1) * P],
                                                        wo_sb[:, kc, :], start=(kc == 0), stop=(kc == KC - 1))
                        last.then_inc(p_mm, 1)
                    if s == 10 and active(i, LAG_B):
                        max_rows(2, 0, bB)
                    if s == 15 and active(i, LAG_B):
                        free(p_out, P_USES, 3)
                        for c in range(TC):
                            for kc in range(KC):
                                last = nc.tensor.matmul(ps_p[:, c * D:(c + 1) * D], cT[:, rB, kc, c * P:(c + 1) * P],
                                                        wv_sb[:, kc, :], start=(kc == 0), stop=(kc == KC - 1))
                        last.then_inc(p_mm, 1)
                    if s == 15 and active(i, LAG_D):
                        pe.wait_ge(z2_done, bD + 1)
                        free(t_out, T_USES, 2)
                        transposes(zr).then_inc(t_mm, 1)
                    if s == 4 and active(i, LAG_D + 1):
                        pe.wait_ge(t_out, uses(i - 1, T_USES, 2) + 1)
                        free(m_out, M_USES, 1)
                        for c in range(TC):
                            for kc in range(KC):
                                last = nc.tensor.matmul(ps_m[:, c * E:(c + 1) * E], z2T[:, kc, c * P:(c + 1) * P],
                                                        rt_sb[:, kc, :], start=(kc == 0), stop=(kc == KC - 1))
                        last.then_inc(m_mm, 1)
                    if s >= 2 and active(i, LAG_C):
                        p_v(s - 2)

            run(pe, step)

        @block.scalar
        def _(act):
            act.wait_ge(const_in, N_CONST)
            nc.scalar.activation(g_tanh[:], g_raw[:], ACT.Tanh).then_inc(gate_ready, 1)
            act.wait_ge(const_dve, DVE_CONSTS)

            def step(i, r, turn):
                bB, bC, bD = i - LAG_B, i - LAG_C, i - LAG_D

                def max_out(k, half, b):
                    act.wait_ge(m_mm, uses(i, M_USES, k) + 1)
                    if due(b):
                        act.wait_ge(m_stack[half], 16 * b)
                    nc.scalar.activation(mrow[:, half, :], ps_m[0:HM, 0:S], ACT.Copy,
                                         scale=1.0 / M_SCALE).then_inc(m_out, 1)

                def biased(k, dst, bias, reused):
                    act.wait_ge(p_mm, uses(i, P_USES, k) + 1)
                    if due(i):
                        act.wait_ge(reused, i)
                    for m in range(KC):
                        last = nc.scalar.activation(dst[:, m, :], ps_p[:, m * S:(m + 1) * S], ACT.Identity,
                                                    bias=bias[:, m:m + 1], scale=QK_SCALE)
                    last.then_inc(p_out, 1)

                for s in range(H + 2):
                    if s < H and active(i, LAG_C):
                        act.wait_ge(k_sc, H * bC + s + 1)
                        n = H * bC + s + 1 - NPT
                        if due(n):
                            act.wait_ge(pv_done, n)
                        nc.scalar.activation(pT[:, s % NPT, :, :], ps_k[s % 2][:].rearrange("p (c q) -> p c q", c=TC),
                                             ACT.Exp, scale=SM_SCALE / M_SCALE).then_inc(p_done, 1)
                    if s == 0 and active(i, 0):
                        act.wait_ge(t_mm, uses(i, T_USES, 0) + 1)
                        if due(i):
                            act.wait_ge(p_mm, uses(i - 1, P_USES, 0) + 1)
                        nc.scalar.copy(zT[:], ps_t[:].rearrange("p (c q) -> p c q", c=KC)).then_inc(t_out, 1)
                    if s == 0 and active(i, LAG_B + 1):
                        max_out(0, 1, bB - 1)
                    if s == 2 and active(i, 0):
                        act.wait_ge(t_mm, uses(i, T_USES, 1) + 1)
                        if due(i - 2):
                            act.wait_ge(p_mm, uses(i - 2, P_USES, 3) + 1)
                        nc.scalar.copy(cT[:, r, :, :], ps_t[:].rearrange("p (c q) -> p c q", c=KC)).then_inc(t_out, 1)
                    if s == 1 and active(i, 0):
                        biased(0, q32, bq_sb, ql_done)
                    if s == 6 and active(i, 0):
                        biased(1, k32, bk_sb, kl_done)
                    if s == 9 and active(i, LAG_B):
                        max_out(2, 0, bB)
                    if s in (8, 17) and active(i, LAG_C):
                        half = 0 if s == 8 else 1
                        act.wait_ge(pv_done, H * bC + HM * (half + 1))
                        if half == 0 and due(bC):
                            act.wait_ge(uc_in, 128 * bC)
                            act.wait_ge(den_out, 32 * bC)
                        nc.scalar.copy(u[:, 2 * half:2 * half + 2, :],
                                       ps_v[:].rearrange("p (g q) -> p g q", g=2)).then_inc(u_done, 1)
                    if s == 16 and active(i, LAG_D):
                        act.wait_ge(t_mm, uses(i, T_USES, 2) + 1)
                        if due(bD):
                            act.wait_ge(m_mm, uses(i, M_USES, 1) + 1)
                        nc.scalar.copy(z2T[:], ps_t[:].rearrange("p (c q) -> p c q", c=KC)).then_inc(t_out, 1)
                    if s == 4 and active(i, LAG_D + 1):
                        b = bD - 1
                        act.wait_ge(ntop_done, b + 1)
                        if due(b):
                            act.wait_ge(w2_done, b)
                        for c in range(TC):
                            last = nc.scalar.activation(ex[:, c, :], top[:, c, :], ACT.Exp,
                                                        bias=ntop[:, c:c + 1], accum_out=esum[:, c:c + 1])
                        last.then_inc(ex_done, 1)

            run(act, step)

        @block.vector
        def _(dve):
            for n in range(NBUF):
                for t in (qa[n], ka[n]):
                    nc.vector.memset(t[0:KROWS, :, :, :].bitcast(F32), 0.0).then_inc(fixed[n], 1)
            dve.wait_ge(const_in, N_CONST)
            dve.wait_ge(const_pool, POOL_CONSTS)
            nc.vector.tensor_scalar(bq_sb[:], bq_raw[:], QK_SCALE, None, ALU.mult).then_inc(const_dve, 1)
            nc.vector.tensor_scalar(bk_sb[:], bk_raw[:], QK_SCALE, None, ALU.mult).then_inc(const_dve, 1)
            for w, raw in ((wq_sb, wq_raw), (wk_sb, wk_raw)):
                for c in range(KC):
                    for half in range(2):
                        last = nc.vector.tensor_copy(
                            w[:, c, half * P:(half + 1) * P].rearrange("p (d m) -> p d m", m=HM),
                            raw[:, c, half * P:(half + 1) * P].rearrange("p (m d) -> p d m", m=HM))
                last.then_inc(const_dve, 1)
            dve.wait_ge(router_tp, 1)
            nc.vector.tensor_copy(rt_sb[:], ps_m[:, 0:KC * E].rearrange("p (c e) -> p c e", c=KC)).then_inc(const_dve, 1)
            dve.wait_ge(gate_ready, 1)
            nc.vector.tensor_scalar(bo_g[:], bo_sb[:], g_tanh[:, 0:1], None, ALU.mult).then_inc(const_dve, 1)

            def row_moments(b, r, turn):
                dve.wait_ge(x_in[r], 16 * (turn + 1))
                for c in range(TC):
                    last = nc.vector.bn_stats(st1[:, c, :], xt[:, r, c, :])
                last.then_inc(st1_done, 1)
                dve.wait_ge(st1_done, b + 1)
                alone(dve)
                for c in range(TC):
                    last = nc.vector.bn_aggr(mv1[:, c, :], st1[:, c, :])
                last.then_inc(mv1_done, 1)

            def normed(b, r):
                dve.wait_ge(rs1_done, b + 1)
                if due(b):
                    dve.wait_ge(t_mm, uses(b - 1, T_USES, 0) + 1)
                for c in range(TC):
                    last = nc.vector.tensor_scalar(z[:, c, :], xt[:, r, c, :], mv1[:, c, 0:1], rs1[:, c:c + 1],
                                                   ALU.subtract, ALU.mult)
                last.then_inc(z_done, 1)

            row_moments(0, 0, 0)
            normed(0, 0)

            def step(i, r, turn):
                bB, bD = i - LAG_B, i - LAG_D
                rB, _ = lagged(r, turn, LAG_B)

                def logits_top(b):
                    logits = ps_m[:, 0:TC * E].rearrange("p (c e) -> p c e", c=TC)
                    dve.wait_ge(m_mm, uses(i, M_USES, 1) + 1)
                    if due(b):
                        dve.wait_ge(ex_done, b)
                    alone(dve)
                    for c in range(TC):
                        last = nc.vector.max(top[:, c, :], logits[:, c, :])
                    last.then_inc(top_done, 1)
                    dve.wait_ge(top_done, b + 1)
                    alone(dve)
                    for c in range(TC):
                        last = nc.vector.max_index(tix[:, c, :], top[:, c, :], logits[:, c, :])
                    last.then_inc(m_out, 1)
                    nc.vector.tensor_scalar(ntop[:], top[:, :, 0], -1.0, None, ALU.mult).then_inc(ntop_done, 1)
                    dve.wait_ge(m_out, uses(i, M_USES, 1) + 1)
                    nc.vector.tensor_copy(tif[:], tix[:, :, 0:K]).then_inc(tif_done, 1)
                    dve.wait_ge(tif_done, b + 1)
                    for k in range(K):
                        last = nc.vector.tensor_tensor(oh[:, k, :, :], wide(iota_e[:], TC),
                                                       tif[:, :, k:k + 1].to_broadcast([P, TC, E]), ALU.is_equal)
                    last.then_inc(oh_done, 1)

                def weights(b):
                    dve.wait_ge(ex_done, b + 1)
                    nc.vector.scalar_tensor_tensor(out=dn0[:], in0=esum[:], scalar=1e-6, in1=ex[:, :, 1],
                                                   op0=ALU.mult, op1=ALU.add).then_inc(dn0_done, 1)
                    dve.wait_ge(dn0_done, b + 1)
                    nc.vector.tensor_scalar(dn[:], dn0[:], 1.0, None, ALU.add).then_inc(dn_done, 1)
                    dve.wait_ge(dn_done, b + 1)
                    nc.vector.reciprocal(w12[:, :, 0], dn[:]).then_inc(w1_done, 1)
                    dve.wait_ge(w1_done, b + 1)
                    nc.vector.tensor_tensor(w12[:, :, 1], ex[:, :, 1], w12[:, :, 0], ALU.mult).then_inc(w2_done, 1)
                    dve.wait_ge(oh_done, b + 1)
                    nc.vector.tensor_tensor(hit[:], oh[:, 0], oh[:, 1], ALU.add).then_inc(hit_done, 1)
                    dve.wait_ge(w2_done, b + 1)
                    for k in range(K):
                        last = nc.vector.tensor_tensor(ow[:, k, :, :], oh[:, k, :, :],
                                                       w12[:, :, k:k + 1].to_broadcast([P, TC, E]), ALU.mult)
                    last.then_inc(ow_done, 1)
                    dve.wait_ge(ow_done, b + 1)
                    nc.vector.tensor_tensor(zr[:, :, D:ROW], ow[:, 0], ow[:, 1], ALU.add).then_inc(wt_done, 1)
                    dve.wait_ge(wt_done, b + 1)
                    dve.wait_ge(hit_done, b + 1)
                    nc.vector.scalar_tensor_tensor(out=wsel[:, :, bass.ts(b, TC)].rearrange("p e t -> p t e"),
                                                   in0=hit[:], scalar=-1.0, in1=zr[:, :, D:ROW],
                                                   op0=ALU.add, op1=ALU.add).then_inc(wsel_done, 1)

                for s in range(H):
                    if active(i, LAG_B):
                        dve.wait_ge(s_mm, H * bB + s + 1)
                        if s == 0 and due(bB):
                            dve.wait_ge(m_mm, uses(i - 1, M_USES, 2) + 1)
                        if s == HM and due(bB):
                            dve.wait_ge(m_mm, uses(i, M_USES, 0) + 1)
                        nc.vector.tensor_reduce(mx[:, :, s], ps_s[s % 2][:].rearrange("p (c k) -> p c k", c=TC),
                                                AX_X, ALU.max).then_inc(mx_done, 1)
                    if s == 4 and active(i, LAG_D + 1):
                        logits_top(bD - 1)
                    if s == 2 and active(i, 0):
                        dve.wait_ge(p_out, uses(i, P_USES, 0) + 1)
                        if due(i):
                            dve.wait_ge(q_stack, 48 * i)
                        nc.vector.tensor_copy(qh[:], q32[:]).then_inc(qh_done, 1)
                    if s == 6 and active(i, LAG_D + 1):
                        weights(bD - 1)
                    if s == 7 and active(i, 0):
                        dve.wait_ge(p_out, uses(i, P_USES, 1) + 1)
                        if due(i):
                            dve.wait_ge(k_stack, 48 * i)
                        nc.vector.tensor_copy(kh[:], k32[:]).then_inc(kh_done, 1)
                    if s == 8 and active(i, LAG_C + 1):
                        b = i - LAG_C - 1
                        dve.wait_ge(den_in, 16 * (b + 1))
                        if due(b):
                            dve.wait_ge(rec_out, 16 * b)
                        nc.vector.reciprocal(rec[:], den[:]).then_inc(rec_done, 1)
                    if s == 10 and active(i, LAG_D):
                        dve.wait_ge(p_mm, uses(i, P_USES, 2) + 1)
                        dve.wait_ge(xb_done, bD + 1)
                        if due(bD):
                            dve.wait_ge(x1_out, 16 * bD)
                        nc.vector.scalar_tensor_tensor(out=x1[:], in0=ps_p[:].rearrange("p (c n) -> p c n", c=TC),
                                                       scalar=g_tanh[:, 0:1], in1=xb[:], op0=ALU.mult,
                                                       op1=ALU.add).then_inc(p_out, 1)
                    if s == 13 and active(i, LAG_D):
                        dve.wait_ge(p_out, uses(i, P_USES, 2) + 1)
                        for c in range(TC):
                            last = nc.vector.bn_stats(st2[:, c, :], x1[:, c, :])
                        last.then_inc(x1_done, 1)
                        dve.wait_ge(x1_done, bD + 1)
                        alone(dve)
                        for c in range(TC):
                            last = nc.vector.bn_aggr(mv2[:, c, :], st2[:, c, :])
                        last.then_inc(mv2_done, 1)
                    if s == 0 and active(i, -1):
                        row_moments(i + 1, (r + 1) % NBUF, turn + (r + 1) // NBUF)
                    if s == 0 and active(i, -1):
                        normed(i + 1, (r + 1) % NBUF)
                    if s == 14 and active(i, LAG_D):
                        dve.wait_ge(rs2_done, bD + 1)
                        if due(bD):
                            dve.wait_ge(rows_out, 16 * bD)
                        for c in range(TC):
                            last = nc.vector.tensor_scalar(zr[:, c, 0:D], x1[:, c, :], mv2[:, c, 0:1], rs2[:, c:c + 1],
                                                           ALU.subtract, ALU.mult)
                        last.then_inc(z2_done, 1)
                    if s == 15 and active(i, LAG_B):
                        dve.wait_ge(p_mm, uses(i, P_USES, 3) + 1)
                        if due(bB - 2):
                            dve.wait_ge(pv_done, H * (bB - 2))
                        nc.vector.tensor_tensor(va[:, rB, :, :, 0:HD],
                                                ps_p[:].rearrange("p (c h d) -> p c h d", c=TC, h=H),
                                                bv_sb[:].rearrange("p (h d) -> p h d", h=H).unsqueeze(1)
                                                .to_broadcast([P, TC, H, HD]), ALU.add).then_inc(p_out, 1)

            run(dve, step)


Z_SCALE = 16.0
W_SCALE = 64.0
H_SCALE = 16.0
CH = 2
CHUNKS = SLOTS // CH
CS = CH * P
PAIRS = FC // 2
GW = KC * F
WCOLS = 2 * GW + FC * D
PREP = 3
OH = 8
OHG = T // OH
OHC = 3


def weight_pieces(n):
    return slice(n * (WCOLS // PREP), (n + 1) * (WCOLS // PREP))


def load_weights(sp, dram, raw, e, n, done):
    sp.dma_start(raw[:, weight_pieces(n)].rearrange("p (c f) -> p c f", c=(KC, KC, FC)[n]),
                 dram[("wg", "wu", "wd")[n]][bass.ds(e, 1)].rearrange("a (c p) f -> p (a c) f", p=P)).then_inc(done, 16)


def experts(nc, dram, wsel, ident, raw):
    out_rows, rows = dram["out_rows"], dram["rows_flat"]
    BITS = range(29, -1, -1)

    with ExitStack() as es:
        def sb(name, shape, dt=F32):
            return es.enter_context(nc.sbuf_tensor(name, shape, dt))

        def pb(name):
            return es.enter_context(nc.psum_tensor(name, [P, 512], F32))

        def sem(name):
            return es.enter_context(nc.semaphore(name))

        wall = sb("wall", [P, N // HD])
        junk = sb("junk", [P, N // HD], F16)
        cnt = sb("cnt", [P, 1], F16)
        cand = sb("cand", [P, 1], I32)
        low = [sb(f"low{n}", [P, 1], I32) for n in range(2)]
        inc = [sb(f"inc{n}", [P, 1], I32) for n in range(2)]
        blk = sb("blk", [P, E, HD], F16)
        tri = sb("tri", [P, P], F16)
        ones = sb("ones", [P, P], F16)
        ones32 = sb("ones32", [P, P])
        tmask = sb("tmask", [T, T], F16)
        esel = sb("esel", [P, E])
        thr_k = sb("thr_k", [P, E])
        thr = sb("thr", [P, E])
        gt = sb("gt", [P, E, T], F16)
        eq = sb("eq", [P, E, T], F16)
        kept = sb("kept", [P, E, T], F16)
        keq = sb("keq", [P, E, T], F16)
        inrank = sb("inrank", [P, E, T], F16)
        before = sb("before", [T, E, T], F16)
        ngt = sb("ngt", [P, E])
        need = sb("need", [P, E])
        pos_i = sb("pos_i", [P, E, T], I32)
        tile_i = sb("tile_i", [P, E, T], I32)
        pin = sb("pin", [P, E, T])
        jin = sb("jin", [P, E, T])
        slot_p = sb("slot_p", [P, P], F16)
        slot_j = sb("slot_j", [P, SLOTS])
        tok_t = sb("tok_t", [P, T])
        part = sb("part", [P, 1])
        spare = sb("spare", [P, 1])
        pe_x = sb("pe_x", [P, T])
        je_x = sb("je_x", [P, T])
        hot = [sb(f"hot{n}", [P, OH, P], F16) for n in range(2)]
        hits = sb("hits", [P, T, SLOTS], F16)
        rhs = [sb(f"rhs{n}", [P, T, 2 * SLOTS], F16) for n in range(2)]
        lst = sb("lst", [P, 2 * SLOTS])
        tok = sb("tok", [P, SLOTS])
        unused = sb("unused", [P, SLOTS])
        gidx = [sb(f"gidx{n}", [P, SLOTS], I32) for n in range(2)]
        sidx = [sb(f"sidx{n}", [P, SLOTS], I32) for n in range(2)]
        g_raw = sb("g2_raw", [P, 1])
        g_tanh = sb("g2_tanh", [P, 1])
        g_out = sb("g_out", [P, 1])
        zero = sb("zero", [P, D])
        wh = [sb(f"wh{n}", [P, WCOLS], F16) for n in range(2)]
        wl = [sb(f"wl{n}", [P, WCOLS], F16) for n in range(2)]
        got = [sb(f"got{n}", [P, CH, ROW]) for n in range(2)]
        zh = [sb(f"zh{n}", [P, KC, CS], F16) for n in range(2)]
        zl = [sb(f"zl{n}", [P, KC, CS], F16) for n in range(2)]
        wsc = [sb(f"wsc{n}", [P, CH, 1]) for n in range(2)]
        sg = [sb(f"sg{n}", [P, 2, CS]) for n in range(2)]
        hs = [sb(f"hs{n}", [P, 2, CS]) for n in range(2)]
        hh = [sb(f"hh{n}", [P, FC, CS], F16) for n in range(2)]
        hl = [sb(f"hl{n}", [P, FC, CS], F16) for n in range(2)]
        y = [sb(f"y{n}", [P, CH, D]) for n in range(2)]

        ps_g = [pb(f"ps_g{n}") for n in range(2)]
        ps_u = [pb(f"ps_u{n}") for n in range(2)]
        ps_y = [pb(f"ps_y{n}") for n in range(2)]
        ps_z = pb("ps_z")
        ps_i = pb("ps_i")

        cp = sem("cp")
        g_in = sem("g_in")
        g_t = sem("g_t")
        zero_out = sem("zero_out")
        w_out = sem("w_out")
        w_in = sem("w_in")
        counted = sem("counted")
        summed = sem("summed")
        stepped = sem("stepped")
        inc_set = sem("inc_set")
        low_set = sem("low_set")
        keq_done = sem("keq_done")
        wl_quarter = sem("wl_quarter")
        thr_k_done = sem("thr_k_done")
        thr_mm = sem("thr_mm")
        thr_done = sem("thr_done")
        gt_done = sem("gt_done")
        eq_done = sem("eq_done")
        tot_mm = sem("tot_mm")
        bef_done = sem("bef_done")
        rank_mm = sem("rank_mm")
        gtot_mm = sem("gtot_mm")
        route = sem("route")
        rhs_step = sem("rhs_step")
        list_step = sem("list_step")
        rhs_done = sem("rhs_done")
        hot_done = sem("hot_done")
        hot_used = sem("hot_used")
        lst_mm = sem("lst_mm")
        idx_done = sem("idx_done")
        raw_in = [sem(f"raw_in_{n}") for n in range(PREP)]
        wh_done = sem("wh_done")
        wl_done = sem("wl_done")
        got_in = [sem(f"got_in{n}") for n in range(2)]
        z_mm = sem("z_mm")
        zh_done = sem("zh_done")
        zl_done = sem("zl_done")
        wsc_done = sem("wsc_done")
        gu_mm = sem("gu_mm")
        sg_done = sem("sg_done")
        hs_done = sem("hs_done")
        hh_done = sem("hh_done")
        hl_done = sem("hl_done")
        y_mm = sem("y_mm")
        y_done = sem("y_done")
        added = sem("added")
        waited = sem("waited2")

        CONSTS = 19

        def alone(eng):
            eng.sem_inc(waited, 1)

        def all_pairs(eng, pair):
            pair(0)
            with eng.Fori(1, E // 2 - 1) as j:
                pair(j)
            pair(E // 2 - 1)

        def later(e):
            return not isinstance(e, int) or e + 1 < E

        block = es.enter_context(nc.Block())

        @block.sync
        def _(sp):
            wflat = dram["wflat"]
            sp.dma_start(wflat.rearrange("(e p t) -> p e t", e=E, p=P), wsel[:]).then_inc(w_out, 16)
            sp.dma_start(g_raw[:], dram["g_ffn"].partition_broadcast(P)).then_inc(g_in, 16)
            sp.wait_ge(w_out, 16)
            sp.dma_start(wall[:], wflat.rearrange("(q n) -> q n", q=P)).then_inc(w_in, 16)
            sp.wait_ge(cp, CONSTS)
            sp.dma_start(out_rows[N:N + SPARE, :], zero[:]).then_inc(zero_out, 16)

            def pair(j):
                for ep in range(2):
                    e = j * 2 + ep
                    for n in range(PREP):
                        if later(e):
                            sp.wait_ge(wh_done, PREP * e + n + 1)
                            alone(sp)
                            sp.wait_ge(wl_done, PREP * e + n + 1)
                            alone(sp)
                            load_weights(sp, dram, raw, e + 1, n, raw_in[n])

            all_pairs(sp, pair)

        @block.gpsimd
        def _(pool):
            fl = dict(allow_small_or_imprecise_dtypes=True)
            sel = nc.gpsimd.affine_select
            nc.gpsimd.memset(blk[:], 1.0).then_inc(cp, 1)
            nc.gpsimd.memset(tri[:], 1.0).then_inc(cp, 1)
            nc.gpsimd.memset(ones[:], 1.0).then_inc(cp, 1)
            nc.gpsimd.memset(ones32[:], 1.0).then_inc(cp, 1)
            nc.gpsimd.memset(tmask[:], 1.0).then_inc(cp, 1)
            nc.gpsimd.memset(esel[:], 0.0).then_inc(cp, 1)
            nc.gpsimd.memset(low[0][:], 0).then_inc(cp, 1)
            nc.gpsimd.memset(cand[:], 1 << BITS[0]).then_inc(cp, 1)
            pool.wait_ge(cp, 8)
            sel(out=blk[:], in_=blk[:], compare_op=ALU.is_ge, fill=0.0, base=0,
                pattern=[[-HD, E], [0, HD]], channel_multiplier=1).then_inc(cp, 1)
            pool.wait_ge(cp, 9)
            sel(out=blk[:], in_=blk[:], compare_op=ALU.is_ge, fill=0.0, base=HD - 1,
                pattern=[[HD, E], [0, HD]], channel_multiplier=-1).then_inc(cp, 1)
            sel(out=esel[:], in_=esel[:], compare_op=ALU.not_equal, fill=1.0, base=0,
                pattern=[[-HD, E]], channel_multiplier=1).then_inc(cp, 1)
            nc.gpsimd.memset(zero[:], 0.0).then_inc(cp, 1)
            sel(out=tri[:], in_=tri[:], compare_op=ALU.is_ge, fill=0.0, base=-1,
                pattern=[[1, P]], channel_multiplier=-1).then_inc(cp, 1)
            pool.wait_ge(cp, 13)
            sel(out=tmask[:], in_=tmask[:], compare_op=ALU.is_ge, fill=0.0, base=-1,
                pattern=[[1, T]], channel_multiplier=-1).then_inc(cp, 1)
            pool.wait_ge(cp, 14)
            nc.gpsimd.iota(slot_p[:], [[1, P]], base=0, channel_multiplier=0, **fl).then_inc(cp, 1)
            nc.gpsimd.iota(slot_j[:], [[1, SLOTS]], base=-int(KEPT), channel_multiplier=0, **fl).then_inc(cp, 1)
            nc.gpsimd.iota(tok_t[:], [[1, T]], base=1, channel_multiplier=0, **fl).then_inc(cp, 1)
            nc.gpsimd.iota(part[:], [[0, 1]], base=0, channel_multiplier=1, **fl).then_inc(cp, 1)
            nc.gpsimd.iota(spare[:], [[0, 1]], base=N + P, channel_multiplier=1, **fl).then_inc(cp, 1)

            def gather(nn, par, e, ep, q):
                if due(nn - 1):
                    pool.wait_ge(z_mm, nn - 1)
                    alone(pool)
                    pool.wait_ge(wsc_done, nn - 1)
                    alone(pool)
                if q == 0:
                    pool.wait_ge(idx_done, e + 1)
                    alone(pool)
                for c in range(CH):
                    t = q * CH + c
                    nc.gpsimd.indirect_dma_start(
                        out=got[par][:, c, :], out_offset=None, in_=rows,
                        in_offset=bass.IndirectOffsetOnAxis(ap=gidx[ep][:, t:t + 1], axis=0)).then_inc(got_in[par], 16)

            def scatter(nn, par, ep, q):
                pool.wait_ge(y_done, nn + 1)
                alone(pool)
                if q == 0 and ep == 0 and not due(nn):
                    pool.wait_ge(zero_out, 16)
                for c in range(CH):
                    t = q * CH + c
                    if due(nn * 2 + c):
                        pool.wait_ge(added, 32 * nn + 16 * c)
                        alone(pool)
                    nc.gpsimd.indirect_dma_start(
                        out=out_rows, out_offset=bass.IndirectOffsetOnAxis(ap=sidx[ep][:, t:t + 1], axis=0),
                        in_=y[par][:, c, :], in_offset=None, compute_op=ALU.add).then_inc(added, 16)

            gather(0, 0, 0, 0, 0)
            gather(1, 1, 0, 0, 1)

            def pair(j):
                for k in range(2 * CHUNKS):
                    ep, q = k // CHUNKS, k % CHUNKS
                    nn, e = j * (2 * CHUNKS) + k, j * 2 + ep
                    if q < CHUNKS - 2:
                        gather(nn + 2, k % 2, e, ep, q + 2)
                    elif later(e):
                        gather(nn + 2, k % 2, e + 1, 1 - ep, q + 2 - CHUNKS)
                    if due(nn):
                        q1 = (q - 1) % CHUNKS
                        scatter(nn - 1, (k - 1) % 2, ep if q else 1 - ep, q1)

            all_pairs(pool, pair)
            scatter(E * CHUNKS - 1, 1, 1, CHUNKS - 1)
            pool.wait_ge(added, 32 * E * CHUNKS)

        @block.tensor
        def _(pe):
            pe.wait_ge(cp, CONSTS)
            for k in range(len(BITS)):
                pe.wait_ge(counted, k + 1)
                nc.tensor.matmul(ps_i[:, 0:1], blk[:].rearrange("p e g -> p (e g)"), cnt[:],
                                 start=True, stop=True).then_inc(summed, 1)
            pe.wait_ge(thr_k_done, 1)
            nc.tensor.matmul(ps_i[:, 0:E], ones32[:], thr_k[:], start=True, stop=True).then_inc(thr_mm, 1)

            def ranks(mask, k):
                for e in range(E):
                    last = nc.tensor.matmul(ps_u[k][0:T, e:e + 1], mask[:, e, :], ones[:, 0:1], start=True, stop=True)
                last.then_inc(tot_mm, 1)
                pe.wait_ge(bef_done, k + 1)
                nc.tensor.matmul(ps_g[k][:], tri[:], mask[:].rearrange("p e t -> p (e t)"), start=True, stop=False)
                nc.tensor.matmul(ps_g[k][:], ones[0:T, :], before[:].rearrange("p e t -> p (e t)"),
                                 start=False, stop=True).then_inc(rank_mm, 1)

            pe.wait_ge(gt_done, 1)
            nc.tensor.matmul(ps_y[0][:], ones[:], gt[:].rearrange("p e t -> p (e t)"), start=True,
                             stop=True).then_inc(gtot_mm, 1)
            pe.wait_ge(eq_done, 1)
            ranks(eq, 0)
            pe.wait_ge(route, 4)
            ranks(kept, 1)

            def slot_sums(e, ep, g, bank_free):
                if g == 0:
                    pe.wait_ge(rhs_done, e + 1)
                    if bank_free:
                        pe.wait_ge(list_step, 3 * e - 2)
                pe.wait_ge(hot_done, OHG * e + g + 1)
                for k in range(OH):
                    t = g * OH + k
                    last = nc.tensor.matmul(ps_i[:, 0:2 * SLOTS], hot[g % 2][:, k, :], rhs[ep][:, t, :],
                                            start=(t == 0), stop=(t == T - 1))
                last.then_inc(hot_used, 1)
                if g == OHG - 1:
                    pe.wait_ge(hot_used, OHG * (e + 1))
                    pe.sem_inc(lst_mm, 1)

            for g in range(OHG):
                slot_sums(0, 0, g, False)

            def slots_to_columns(nn, par):
                pe.wait_ge(got_in[par], 32 * (nn // 2 + 1) if isinstance(nn, int) else 16 * (nn - par) + 32)
                if due(nn):
                    pe.wait_ge(zl_done, nn)
                for kc in range(KC):
                    for c in range(CH):
                        last = nc.tensor.transpose(ps_z[:, kc * CS + c * P:kc * CS + (c + 1) * P],
                                                   got[par][:, c, kc * P:(kc + 1) * P], ident[:])
                last.then_inc(z_mm, 1)

            def up(nn, par, ep, m):
                n = PAIRS * nn + m - 1
                for bank, first, free in ((ps_g[m % 2], 0, sg_done), (ps_u[m % 2], GW, hs_done)):
                    if due(n):
                        pe.wait_ge(free, n)
                    for h in range(2):
                        f = 2 * m + h
                        terms = [(w, zz, c) for c in range(KC)
                                 for w, zz in ((wh[ep], zh[par]), (wh[ep], zl[par]), (wl[ep], zh[par]))]
                        for k, (w, zz, c) in enumerate(terms):
                            a = first + c * F + f * P
                            last = nc.tensor.matmul(bank[:, h * CS:(h + 1) * CS], w[:, a:a + P], zz[:, c, :],
                                                    start=(k == 0), stop=(k == len(terms) - 1))
                last.then_inc(gu_mm, 1)

            def down(nn, par, ep):
                pe.wait_ge(hl_done, PAIRS * (nn + 1))
                if due(nn - 1):
                    pe.wait_ge(y_done, nn - 1)
                for c in range(CH):
                    terms = [(hx, w, f) for f in range(FC)
                             for hx, w in ((hh[par], wh[ep]), (hl[par], wh[ep]), (hh[par], wl[ep]))]
                    for k, (hx, w, f) in enumerate(terms):
                        a = 2 * GW + f * D
                        last = nc.tensor.matmul(ps_y[par][:, c * D:(c + 1) * D], hx[:, f, c * P:(c + 1) * P],
                                                w[:, a:a + D], start=(k == 0), stop=(k == len(terms) - 1))
                last.then_inc(y_mm, 1)

            slots_to_columns(0, 0)

            def next_slots(e, ep, g):
                if g < OHG and later(e):
                    slot_sums(e + 1, 1 - ep, g, True)

            def pair(j):
                for k in range(2 * CHUNKS):
                    ep, q, par = k // CHUNKS, k % CHUNKS, k % 2
                    nn, e = j * (2 * CHUNKS) + k, j * 2 + ep
                    pe.wait_ge(zl_done, nn + 1)
                    if q == 0:
                        pe.wait_ge(wl_done, PREP * (e + 1))
                    up(nn, par, ep, 0)
                    up(nn, par, ep, 1)
                    if q < CHUNKS - 1 or later(e):
                        slots_to_columns(nn + 1, 1 - par)
                    if due(nn):
                        down(nn - 1, 1 - par, ep if q else 1 - ep)
                    next_slots(e, ep, OHC * q)
                    up(nn, par, ep, 2)
                    next_slots(e, ep, OHC * q + 1)
                    up(nn, par, ep, 3)
                    next_slots(e, ep, OHC * q + 2)

            all_pairs(pe, pair)
            down(E * CHUNKS - 1, 1, 1)

        @block.scalar
        def _(act):
            act.wait_ge(g_in, 16)
            nc.scalar.activation(g_tanh[:], g_raw[:], ACT.Tanh).then_inc(g_t, 1)

            def split_high(e, ep, n):
                if due(e):
                    act.wait_ge(raw_in[n], 16 * e)
                if n == 0 and due(e - 1):
                    act.wait_ge(y_mm, CHUNKS * (e - 1))
                nc.scalar.activation(wh[ep][:, weight_pieces(n)], raw[:, weight_pieces(n)], ACT.Copy,
                                     scale=W_SCALE).then_inc(wh_done, 1)

            def tokens_high(nn, par):
                act.wait_ge(z_mm, nn + 1)
                if due(nn - 1):
                    act.wait_ge(gu_mm, PAIRS * (nn - 1))
                nc.scalar.activation(zh[par][:], ps_z[:].rearrange("p (c q) -> p c q", c=KC), ACT.Copy,
                                     scale=Z_SCALE).then_inc(zh_done, 1)

            for n in range(PREP):
                split_high(0, 0, n)
            tokens_high(0, 0)

            def hidden_high(nn, par, m):
                act.wait_ge(hs_done, PAIRS * nn + m + 1)
                if m == 0 and due(nn - 1):
                    act.wait_ge(y_mm, nn - 1)
                nc.scalar.copy(hh[par][:, 2 * m:2 * m + 2, :], hs[m % 2][:]).then_inc(hh_done, 1)

            def pair(j):
                for k in range(2 * CHUNKS):
                    ep, q, par = k // CHUNKS, k % CHUNKS, k % 2
                    nn, e = j * (2 * CHUNKS) + k, j * 2 + ep
                    for m in range(PAIRS):
                        act.wait_ge(gu_mm, PAIRS * nn + m + 1)
                        n = PAIRS * nn + m - 1
                        if due(n):
                            act.wait_ge(hs_done, n)
                        nc.scalar.activation(sg[m % 2][:], ps_g[m % 2][:].rearrange("p (c q) -> p c q", c=2), ACT.Silu,
                                             scale=1.0 / (Z_SCALE * W_SCALE)).then_inc(sg_done, 1)
                        if m:
                            hidden_high(nn, par, m - 1)
                        if m == PAIRS - 1:
                            hidden_high(nn, par, m)
                        if m == 1 and (q < CHUNKS - 1 or later(e)):
                            tokens_high(nn + 1, 1 - par)
                        if m == 2 and q < PREP and later(e):
                            split_high(e + 1, 1 - ep, q)

            all_pairs(act, pair)

        @block.vector
        def _(dve):
            dve.wait_ge(cp, CONSTS)
            dve.wait_ge(g_t, 1)
            nc.vector.tensor_scalar(g_out[:], g_tanh[:], 1.0 / (H_SCALE * W_SCALE), None, ALU.mult).then_inc(g_t, 1)

            def split_low(e, ep, n):
                dve.wait_ge(wh_done, PREP * e + n + 1)
                cols = weight_pieces(n)
                nc.vector.scalar_tensor_tensor(out=wl[ep][:, cols], in0=raw[:, cols], scalar=W_SCALE, in1=wh[ep][:, cols],
                                               op0=ALU.mult, op1=ALU.subtract).then_inc(wl_done, 1)

            dve.wait_ge(w_in, 16)
            for k, bit in enumerate(BITS):
                if k:
                    dve.wait_ge(stepped, k)
                nc.vector.tensor_scalar(junk[:], wall[:], cand[:].bitcast(F32), None, ALU.is_ge, ALU.add,
                                        accum_out=cnt[:]).then_inc(counted, 1)
                if k:
                    nc.vector.tensor_tensor(low[k % 2][:], low[(k + 1) % 2][:], inc[(k + 1) % 2][:],
                                            ALU.bitwise_or).then_inc(low_set, 1)
                if k < 4 * PREP:
                    n, quarter = k // 4, k % 4
                    dve.wait_ge(wh_done, n + 1)
                    width = WCOLS // PREP // 4
                    cols = slice((4 * n + quarter) * width, (4 * n + quarter + 1) * width)
                    nc.vector.scalar_tensor_tensor(out=wl[0][:, cols], in0=raw[:, cols], scalar=W_SCALE, in1=wh[0][:, cols],
                                                   op0=ALU.mult, op1=ALU.subtract).then_inc(wl_quarter, 1)
                    if quarter == 3:
                        dve.wait_ge(wl_quarter, k + 1)
                        dve.sem_inc(wl_done, 1)
                dve.wait_ge(summed, k + 1)
                nc.vector.tensor_scalar(inc[k % 2][:], ps_i[:, 0:1], float(CAP), float(1 << bit), ALU.is_ge,
                                        ALU.mult).then_inc(inc_set, 1)
                dve.wait_ge(inc_set, k + 1)
                if k:
                    dve.wait_ge(low_set, k)
                nc.vector.scalar_tensor_tensor(out=cand[:], in0=inc[k % 2][:], scalar=(1 << bit) >> 1, in1=low[k % 2][:],
                                               op0=ALU.bitwise_or, op1=ALU.bitwise_or).then_inc(stepped, 1)
            dve.wait_ge(stepped, len(BITS))
            nc.vector.tensor_scalar(thr_k[:], esel[:], cand[:].bitcast(F32), None, ALU.mult).then_inc(thr_k_done, 1)
            dve.wait_ge(thr_mm, 1)
            nc.vector.tensor_copy(thr[:], ps_i[:, 0:E]).then_inc(thr_done, 1)
            dve.wait_ge(thr_done, 1)
            thr_b = thr[:].unsqueeze(2).to_broadcast([P, E, T])
            nc.vector.tensor_tensor(gt[:], wsel[:], thr_b, ALU.is_gt).then_inc(gt_done, 1)
            nc.vector.tensor_tensor(eq[:], wsel[:], thr_b, ALU.is_equal).then_inc(eq_done, 1)

            def tiles_before(k):
                dve.wait_ge(tot_mm, k + 1)
                nc.vector.tensor_tensor(before[:], ps_u[k][0:T, 0:E].unsqueeze(2).to_broadcast([T, E, T]),
                                        tmask[:].unsqueeze(1).to_broadcast([T, E, T]), ALU.mult).then_inc(bef_done, 1)

            tiles_before(0)
            dve.wait_ge(gtot_mm, 1)
            nc.vector.tensor_reduce(ngt[:], ps_y[0][:].rearrange("p (e t) -> p e t", e=E), AX_X, ALU.add).then_inc(route, 1)
            dve.wait_ge(route, 1)
            nc.vector.tensor_scalar(need[:], ngt[:], -1.0, float(CAP), ALU.mult, ALU.add).then_inc(route, 1)
            dve.wait_ge(route, 2)
            dve.wait_ge(rank_mm, 1)
            nc.vector.tensor_tensor(inrank[:], ps_g[0][:].rearrange("p (e t) -> p e t", e=E),
                                    need[:].unsqueeze(2).to_broadcast([P, E, T]), ALU.is_lt).then_inc(route, 1)
            dve.wait_ge(route, 3)
            nc.vector.tensor_tensor(keq[:], inrank[:], eq[:], ALU.mult).then_inc(keq_done, 1)
            dve.wait_ge(keq_done, 1)
            nc.vector.tensor_tensor(kept[:], gt[:], keq[:], ALU.add).then_inc(route, 1)
            tiles_before(1)
            dve.wait_ge(rank_mm, 2)
            pos = ps_g[1][:].rearrange("p (e t) -> p e t", e=E)
            nc.vector.tensor_copy(pos_i[:], pos).then_inc(route, 1)
            dve.wait_ge(route, 5)
            nc.vector.tensor_scalar(tile_i[:], pos_i[:], 7, None, ALU.arith_shift_right).then_inc(route, 1)
            dve.wait_ge(route, 6)
            nc.vector.scalar_tensor_tensor(out=pin[:], in0=tile_i[:], scalar=-float(P), in1=pos, op0=ALU.mult,
                                           op1=ALU.add).then_inc(route, 1)
            nc.vector.scalar_tensor_tensor(out=jin[:], in0=kept[:], scalar=-KEPT, in1=tile_i[:], op0=ALU.mult,
                                           op1=ALU.add).then_inc(route, 1)
            dve.wait_ge(route, 8)

            def slot_rhs(e, ep):
                if due(e):
                    dve.wait_ge(hot_used, OHG * e)
                nc.vector.tensor_copy(pe_x[:], pin[:, bass.ds(e, 1), :].rearrange("p a t -> p (a t)"))
                nc.vector.tensor_copy(je_x[:], jin[:, bass.ds(e, 1), :].rearrange("p a t -> p (a t)")).then_inc(rhs_step, 1)
                dve.wait_ge(rhs_step, 2 * e + 1)
                nc.vector.tensor_tensor(hits[:], je_x[:].unsqueeze(2).to_broadcast([P, T, SLOTS]),
                                        slot_j[:].unsqueeze(1).to_broadcast([P, T, SLOTS]), ALU.is_equal).then_inc(rhs_step, 1)
                dve.wait_ge(rhs_step, 2 * e + 2)
                nc.vector.tensor_tensor(rhs[ep][:, :, 0:SLOTS], hits[:], tok_t[:].unsqueeze(2).to_broadcast([P, T, SLOTS]),
                                        ALU.mult)
                nc.vector.tensor_scalar(rhs[ep][:, :, SLOTS:], hits[:], part[:, 0:1], None, ALU.mult).then_inc(rhs_done, 1)

            def hot_group(e, g):
                n = OHG * e + g - 1
                if due(n):
                    dve.wait_ge(hot_used, n)
                nc.vector.tensor_tensor(hot[g % 2][:], slot_p[:].unsqueeze(1).to_broadcast([P, OH, P]),
                                        pe_x[:, g * OH:(g + 1) * OH].unsqueeze(2).to_broadcast([P, OH, P]),
                                        ALU.is_equal).then_inc(hot_done, 1)

            def slot_indices(e, ep):
                dve.wait_ge(lst_mm, e + 1)
                nc.vector.tensor_copy(lst[:], ps_i[:, 0:2 * SLOTS]).then_inc(list_step, 1)
                dve.wait_ge(list_step, 3 * e + 1)
                nc.vector.scalar_tensor_tensor(out=tok[:], in0=lst[:, 0:SLOTS], scalar=float(P), in1=lst[:, SLOTS:],
                                               op0=ALU.mult, op1=ALU.add).then_inc(list_step, 1)
                nc.vector.tensor_scalar(unused[:], lst[:, 0:SLOTS], 0.0, spare[:, 0:1], ALU.is_equal,
                                        ALU.mult).then_inc(list_step, 1)
                dve.wait_ge(list_step, 3 * e + 3)
                if due(e - 1):
                    dve.wait_ge(added, 32 * CHUNKS * (e - 1))
                nc.vector.tensor_scalar(gidx[ep][:], tok[:], -float(P), 0.0, ALU.add, ALU.max)
                nc.vector.scalar_tensor_tensor(out=sidx[ep][:], in0=tok[:], scalar=-float(P), in1=unused[:], op0=ALU.add,
                                               op1=ALU.add).then_inc(idx_done, 1)

            slot_rhs(0, 0)
            dve.wait_ge(rhs_done, 1)
            for g in range(OHG):
                hot_group(0, g)
            slot_indices(0, 0)

            def tokens_low(nn, par):
                dve.wait_ge(zh_done, nn + 1)
                nc.vector.scalar_tensor_tensor(out=zl[par][:], in0=ps_z[:].rearrange("p (c q) -> p c q", c=KC),
                                               scalar=Z_SCALE, in1=zh[par][:], op0=ALU.mult,
                                               op1=ALU.subtract).then_inc(zl_done, 1)

            def slot_weights(nn, par, e):
                if due(nn - 1):
                    dve.wait_ge(y_done, nn - 1)
                nc.vector.tensor_scalar(wsc[par][:], got[par][:, :, bass.ds(e + D, 1)], g_out[:, 0:1], None,
                                        ALU.mult).then_inc(wsc_done, 1)

            tokens_low(0, 0)
            slot_weights(0, 0, 0)

            def hidden_low(nn, par, m):
                dve.wait_ge(hh_done, PAIRS * nn + m + 1)
                nc.vector.tensor_tensor(hl[par][:, 2 * m:2 * m + 2, :], hs[m % 2][:], hh[par][:, 2 * m:2 * m + 2, :],
                                        ALU.subtract).then_inc(hl_done, 1)

            def weigh(nn, par):
                dve.wait_ge(y_mm, nn + 1)
                if due(nn - 1):
                    dve.wait_ge(added, 32 * (nn - 1))
                for c in range(CH):
                    last = nc.vector.tensor_scalar(y[par][:, c, :], ps_y[par][:, c * D:(c + 1) * D], wsc[par][:, c, :],
                                                   None, ALU.mult)
                last.then_inc(y_done, 1)

            def pair(j):
                for k in range(2 * CHUNKS):
                    ep, q, par = k // CHUNKS, k % CHUNKS, k % 2
                    nn, e = j * (2 * CHUNKS) + k, j * 2 + ep
                    for m in range(PAIRS):
                        n = PAIRS * nn + m + 1
                        dve.wait_ge(sg_done, n)
                        if due(n - 2):
                            dve.wait_ge(hl_done, n - 2)
                        nc.vector.scalar_tensor_tensor(out=hs[m % 2][:], in0=ps_u[m % 2][:].rearrange("p (c q) -> p c q", c=2),
                                                       scalar=H_SCALE / (Z_SCALE * W_SCALE), in1=sg[m % 2][:],
                                                       op0=ALU.mult, op1=ALU.mult).then_inc(hs_done, 1)
                        if m == 0 and q == 0 and later(e):
                            slot_rhs(e + 1, 1 - ep)
                        if m < OHC and OHC * q + m < OHG and later(e):
                            hot_group(e + 1, OHC * q + m)
                        if m:
                            hidden_low(nn, par, m - 1)
                        if m == 1 and (q < CHUNKS - 1 or later(e)):
                            tokens_low(nn + 1, 1 - par)
                        if m == 2 and due(nn):
                            weigh(nn - 1, 1 - par)
                        if m == 2 and (q < CHUNKS - 1 or later(e)):
                            slot_weights(nn + 1, 1 - par, e if q < CHUNKS - 1 else e + 1)
                        if m == 3 and q < PREP and later(e):
                            split_low(e + 1, 1 - ep, q)
                        if m == PAIRS - 1:
                            hidden_low(nn, par, m)
                            if q == (OHG - 1) // OHC and later(e):
                                slot_indices(e + 1, 1 - ep)

            all_pairs(dve, pair)
            weigh(E * CHUNKS - 1, 1)


def block_program(nc, x, ctx, g_xattn, g_ffn, wq, bq, wk, bk, wv, bv, wo, bo, router, wg, wu, wd, out):
    dram = {
        "x": x.rearrange("b (c p) n -> (b c) p n", p=P), "ctx": ctx.rearrange("b (c p) n -> (b c) p n", p=P),
        "wq": wq, "bq": bq, "wk": wk, "bk": bk, "wv": wv, "bv": bv, "wo": wo, "bo": bo,
        "g_xattn": g_xattn, "g_ffn": g_ffn, "router": router, "wg": wg, "wu": wu, "wd": wd,
        "out": out.rearrange("(t p) n -> t p n", p=P), "out_rows": out,
    }
    dram["rows_flat"] = nc.dram_tensor("rows", [N, ROW], F32).ap()
    dram["rows"] = dram["rows_flat"].rearrange("(t p) n -> t p n", p=P)
    dram["rsum"] = nc.dram_tensor("rsum", [H * S], F32).ap()
    dram["rinv"] = nc.dram_tensor("rinv", [H * S], F32).ap()
    dram["wflat"] = nc.dram_tensor("wflat", [E * P * T], F32).ap()
    with ExitStack() as es:
        wsel = es.enter_context(nc.sbuf_tensor("wsel", [P, E, T], F32))
        ident = es.enter_context(nc.sbuf_tensor("ident", [P, P], F32))
        raw = es.enter_context(nc.sbuf_tensor("raw", [P, WCOLS], F32))
        attention(nc, dram, wsel, ident, raw)
        experts(nc, dram, wsel, ident, raw)


_INS = ["x", "ctx_1024", "g_xattn", "g_ffn", "L0_xattn_Wq", "L0_xattn_bq", "L0_xattn_Wk", "L0_xattn_bk",
        "L0_xattn_Wv", "L0_xattn_bv", "L0_xattn_Wo", "L0_xattn_bo", "L0_ffn_router_w", "L0_ffn_wg",
        "L0_ffn_wu", "L0_ffn_wd"]


def kernel(**inputs):
    import numpy as np
    import concourse.bacc as bacc
    from concourse.bass_utils import run_bass_kernel_spmd

    nc = bacc.Bacc("TRN2", target_bir_lowering=False, num_devices=1)
    arrays, args = {}, []
    for name in _INS:
        a = np.ascontiguousarray(inputs[name])
        arrays[f"in_{name}"] = a
        args.append(nc.dram_tensor(f"in_{name}", a.shape, mybir.dt.from_np(a.dtype), kind="ExternalInput").ap())
    args.append(nc.dram_tensor("out_rows", (N + SPARE, D), F32, kind="ExternalOutput").ap())
    block_program(nc, *args)
    got = run_bass_kernel_spmd(nc, [arrays], core_ids=[0]).results[0]["out_rows"]
    return got[:N].reshape(B, S, D)
```
